# Optimizing a Trainium2 kernel written in Bass

```python
import numpy as np
import jax
import jax.numpy as jnp

def _softmax(x, axis=-1):
    return jax.nn.softmax(x, axis=axis)

def _gelu(x):
    return jax.nn.gelu(x, approximate=True)

def _silu(x):
    return jax.nn.silu(x)

def _sigmoid(x):
    return jax.nn.sigmoid(x)

def _layernorm(x, axis=-1, eps=1e-05):
    m = jnp.mean(x, axis=axis, keepdims=True)
    v = jnp.var(x, axis=axis, keepdims=True)
    return (x - m) / jnp.sqrt(v + eps)

def _scatter_add(tgt, idx, src, axis=0):
    return tgt.at[idx].add(src)

def _segment_sum(src, seg, n):
    return jax.ops.segment_sum(src, seg, n)
kernel_name = 'mk_adj_ffn_d1_adj_r2_e08331'

def setup_inputs(seed: int=0):
    np.random.seed(seed)
    _w = jnp.asarray

    def _rec_inputs():
        import jax
        import jax.numpy as jnp
        _gk = jax.random.key(seed)
        x = -0.0002928 + 1 * jax.random.normal(jax.random.fold_in(_gk, 1), (16, 512, 128), jnp.float32)
        _a = jax.random.bernoulli(jax.random.fold_in(_gk, 2), 0.0078125, (16, 512, 512))
        _a = jnp.logical_or(_a, jnp.swapaxes(_a, -1, -2))
        _a = jnp.logical_or(_a, jnp.eye(512, dtype=bool))
        adj = _a.astype(jnp.int32)
        return (x, adj)
    x, adj = _rec_inputs()

    def _L0_gnn_setup():
        import jax, jax.numpy as jnp
        import numpy as np
        key = jax.random.key(seed)
        k1, k2, k3, k4 = jax.random.split(key, 4)
        B, N, F, U = (8, 1024, 128, 128)
        x = jax.random.normal(k1, (B, N, F), dtype=jnp.float32)
        adj = jax.random.randint(k2, (B, N, N), 0, 2, dtype=jnp.int32)
        W_msg = jax.random.normal(k3, (F, U), dtype=jnp.float32) / np.sqrt(F)
        W_upd = jax.random.normal(k4, (F, U), dtype=jnp.float32) / np.sqrt(F)
        bias = jnp.zeros((U,), dtype=jnp.float32)
        return {'x': x, 'adj': adj, 'W_msg': W_msg, 'W_upd': W_upd, 'bias': bias}
    _L0_gnn_all = _L0_gnn_setup()
    _L0_gnn_in = {k: v for k, v in _L0_gnn_all.items() if k in ('W_msg', 'W_upd', 'bias')}
    del _L0_gnn_all

    def _L0_ffn_setup():
        import jax, jax.numpy as jnp
        import numpy as np
        DIM = 128
        HEADS = 8
        NUM_KEYS = 128
        NUM_KV = NUM_KEYS ** 2
        PK_TOPK = 16
        FINAL_TOPK = 16
        DIM_KEY = DIM // 2
        P = 2

        def _pk(x, Wq_pk, pk_keys):
            b, n, _ = x.shape
            q = (x @ Wq_pk).reshape(b, n, P, HEADS, DIM_KEY).transpose(2, 0, 1, 3, 4)
            sim = jnp.einsum('pbnhd,pkhd->pbnhk', q, pk_keys)
            scores, idx = jax.lax.top_k(sim, PK_TOPK)
            idx0 = idx[0]
            idx1 = idx[1] * NUM_KEYS
            index = (idx0[..., :, None] + idx1[..., None, :]).reshape(b, n, HEADS, PK_TOPK * PK_TOPK)
            score = (scores[0][..., :, None] + scores[1][..., None, :]).reshape(b, n, HEADS, PK_TOPK * PK_TOPK)
            final_scores, pk_idx = jax.lax.top_k(score, FINAL_TOPK)
            final_indices = jnp.take_along_axis(index, pk_idx, axis=-1)
            final_scores = jax.nn.softmax(final_scores, axis=-1)
            return (final_scores, final_indices)
        key = jax.random.key(seed)
        ks = jax.random.split(key, 7)
        b, n = (2, 512)
        std = 0.02
        x = jax.random.normal(ks[0], (b, n, DIM), dtype=jnp.float32)
        Wq_pk = jax.random.normal(ks[1], (DIM, P * HEADS * DIM_KEY), dtype=jnp.float32) * std
        pk_keys = jax.random.normal(ks[2], (P, NUM_KEYS, HEADS, DIM_KEY), dtype=jnp.float32) * std
        Wq = jax.random.normal(ks[3], (DIM, HEADS * DIM), dtype=jnp.float32) * std
        keys_table = jax.random.normal(ks[4], (NUM_KV * HEADS, DIM), dtype=jnp.float32) * std
        values_table = jax.random.normal(ks[5], (NUM_KV * HEADS, DIM), dtype=jnp.float32) * std
        Wo = jax.random.normal(ks[6], (DIM * HEADS, DIM), dtype=jnp.float32) * std
        return {'x': x, 'Wq_pk': Wq_pk, 'pk_keys': pk_keys, 'Wq': Wq, 'keys_table': keys_table, 'values_table': values_table, 'Wo': Wo}
    _L0_ffn_all = _L0_ffn_setup()
    _L0_ffn_in = {k: v for k, v in _L0_ffn_all.items() if k in ('Wq_pk', 'pk_keys', 'Wq', 'keys_table', 'values_table', 'Wo')}
    del _L0_ffn_all
    return {'x': x, 'adj': adj, 'L0_gnn_W_msg': _L0_gnn_in['W_msg'], 'L0_gnn_W_upd': _L0_gnn_in['W_upd'], 'L0_gnn_bias': _L0_gnn_in['bias'], 'L0_ffn_Wq_pk': _L0_ffn_in['Wq_pk'], 'L0_ffn_pk_keys': _L0_ffn_in['pk_keys'], 'L0_ffn_Wq': _L0_ffn_in['Wq'], 'L0_ffn_keys_table': _L0_ffn_in['keys_table'], 'L0_ffn_values_table': _L0_ffn_in['values_table'], 'L0_ffn_Wo': _L0_ffn_in['Wo']}

def reference(x, adj, L0_gnn_W_msg, L0_gnn_W_upd, L0_gnn_bias, L0_ffn_Wq_pk, L0_ffn_pk_keys, L0_ffn_Wq, L0_ffn_keys_table, L0_ffn_values_table, L0_ffn_Wo):
    import jax
    import jax.numpy as jnp

    def _L0_gnn_ref(x, adj, W_msg, W_upd, bias):
        import jax, jax.numpy as jnp
        import numpy as np
        a = adj.astype(x.dtype)
        h = jnp.einsum('bnf,fu->bnu', x, W_msg)
        msg_sum = jnp.einsum('bij,biu->bju', a, h)
        deg = jnp.sum(a, axis=1)
        messages = jnp.where(deg[..., None] > 0, msg_sum / jnp.maximum(deg, 1.0)[..., None], 0.0)
        out = jnp.einsum('bnf,fu->bnu', x, W_upd) + messages + bias
        return jax.nn.relu(out)

    def _L0_ffn_ref(x, Wq_pk, pk_keys, Wq, keys_table, values_table, Wo):
        import jax, jax.numpy as jnp
        import numpy as np
        DIM = 128
        HEADS = 8
        NUM_KEYS = 128
        NUM_KV = NUM_KEYS ** 2
        PK_TOPK = 16
        FINAL_TOPK = 16
        DIM_KEY = DIM // 2
        P = 2

        def _pk(x, Wq_pk, pk_keys):
            b, n, _ = x.shape
            q = (x @ Wq_pk).reshape(b, n, P, HEADS, DIM_KEY).transpose(2, 0, 1, 3, 4)
            sim = jnp.einsum('pbnhd,pkhd->pbnhk', q, pk_keys)
            scores, idx = jax.lax.top_k(sim, PK_TOPK)
            idx0 = idx[0]
            idx1 = idx[1] * NUM_KEYS
            index = (idx0[..., :, None] + idx1[..., None, :]).reshape(b, n, HEADS, PK_TOPK * PK_TOPK)
            score = (scores[0][..., :, None] + scores[1][..., None, :]).reshape(b, n, HEADS, PK_TOPK * PK_TOPK)
            final_scores, pk_idx = jax.lax.top_k(score, FINAL_TOPK)
            final_indices = jnp.take_along_axis(index, pk_idx, axis=-1)
            final_scores = jax.nn.softmax(final_scores, axis=-1)
            return (final_scores, final_indices)
        b, n, d = x.shape
        q = (x @ Wq).reshape(b, n, HEADS, DIM) * DIM ** (-0.5)
        kv_scores, indices = _pk(x, Wq_pk, pk_keys)
        offsets = jnp.arange(HEADS, dtype=indices.dtype) * NUM_KV
        ind = indices + offsets[None, None, :, None]
        k = jnp.einsum('bnhk,bnhkd->bnhd', kv_scores, keys_table[ind])
        v = jnp.einsum('bnhk,bnhkd->bnhd', kv_scores, values_table[ind])
        sim = jnp.einsum('bihd,bjhd->bhij', q, k)
        neg = -jnp.finfo(sim.dtype).max
        causal = jnp.tril(jnp.ones((n, n), dtype=bool))
        sim = jnp.where(causal, sim, neg)
        attn = jax.nn.softmax(sim, axis=-1)
        out = jnp.einsum('bhij,bjhd->bhid', attn, v)
        out = out.transpose(0, 2, 1, 3).reshape(b, n, HEADS * DIM)
        return out @ Wo
    x = x + _L0_gnn_ref(_layernorm(x, axis=-1), adj, L0_gnn_W_msg, L0_gnn_W_upd, L0_gnn_bias)
    x = x + _L0_ffn_ref(_layernorm(x, axis=-1), L0_ffn_Wq_pk, L0_ffn_pk_keys, L0_ffn_Wq, L0_ffn_keys_table, L0_ffn_values_table, L0_ffn_Wo)
    return x

_drawn_inputs = setup_inputs


def setup_inputs(seed=0):
    import zlib

    import numpy as np

    out = dict(_drawn_inputs(seed))
    spreads = {'L0_gnn_bias': (0.0, 0.1)}
    factors = {'L0_ffn_Wq_pk': 8.0,
     'L0_ffn_pk_keys': 8.0,
     'L0_ffn_Wq': 64.0,
     'L0_ffn_keys_table': 64.0,
     'L0_ffn_values_table': 8.0,
     'L0_ffn_Wo': 8.0}
    for name, (base, spread) in spreads.items():
        noise = np.random.default_rng([zlib.crc32(name.encode()), seed]).standard_normal(out[name].shape)
        drawn = base * np.exp(spread * noise) if base else spread * noise
        out[name] = jnp.asarray(drawn.astype(out[name].dtype))
    for name, factor in factors.items():
        out[name] = (out[name] * factor).astype(out[name].dtype)
    return out
```

```python
from concourse import bass, mybir
from concourse.alu_op_type import AluOpType as ALU

F32 = mybir.dt.float32
U32 = mybir.dt.uint32
I32 = mybir.dt.int32
ACT = mybir.ActivationFunctionType
AX = mybir.AxisListType

P = 128
B, N, D = 16, 512, 128
T = N // P
H = 8
SIDES, NKEYS, DKEY = 2, 128, 64
TOPK = 16
ROWS = NKEYS * NKEYS
STEPS = B * H
RUN = [TOPK // (i + 1) for i in range(TOPK)]
START = [sum(RUN[:i]) for i in range(TOPK)]
NCAND = sum(RUN)
GROUPS = []
for _i in range(TOPK):
    if GROUPS and RUN[GROUPS[-1][0]] == RUN[_i]:
        GROUPS[-1][1] += 1
    else:
        GROUPS.append([_i, 1])
LOWEST = -3.4e38
EPS = 1e-5
SCALE = float(D) ** -0.5


def program(nc, x, adj, w_msg, w_upd, bias, wqpk_t, keys_t, wq, table, wo, out):
    def sb(name, shape, dt=F32):
        return nc.alloc_sbuf_tensor(name, shape, dt)

    def pb(name):
        return nc.alloc_psum_tensor(name, [P, 512], F32)

    sem = nc.alloc_semaphore

    w_hu = sb("w_hu", [P, 2 * D])
    bias_all = sb("bias_all", [P, D])
    wqpk_sb = sb("wqpk_sb", [DKEY, SIDES * H * D])
    keys_sb = sb("keys_sb", [DKEY, SIDES * H * NKEYS])
    w_sim = sb("w_sim", [P, H * SIDES * NKEYS])
    wq_sb = sb("wq_sb", [P, H * D])
    wq_head = sb("wq_head", [P, D])
    wo_sb = sb("wo_sb", [P, H, D])
    ident = sb("ident", [P, P])
    mask = sb("mask", [P, N])
    iota_i = sb("iota_i", [P, NCAND], I32)
    iota_f = sb("iota_f", [P, NCAND])
    head_row = sb("head_row", [P, H])
    x_in = sb("x_in", [P, T, D])
    adj_i = sb("adj_i", [P, T, N], I32)
    adj_f = sb("adj_f", [P, T, N])
    stats = sb("stats", [P, T, 6])
    meanvar = sb("meanvar", [P, T, 2])
    var = sb("var", [P, T])
    sd = sb("sd", [P, T])
    rstd = sb("rstd", [P, T])
    rstd2 = sb("rstd2", [P, T])
    xn = sb("xn", [P, T, D])
    xnT = sb("xnT", [P, N])
    hu = sb("hu", [P, T, 2 * D + 1])
    deg = sb("deg", [P, T])
    degpos = sb("degpos", [P, T])
    upd = sb("upd", [P, T, D])
    x2 = sb("x2", [P, T, D])
    x2nT = sb("x2nT", [P, N])
    sim = sb("sim", [P, T, SIDES * NKEYS])
    sim_rest = sb("sim_rest", [P, 2 * SIDES, NKEYS])
    top_v = sb("top_v", [P, T, SIDES, TOPK])
    top_i = sb("top_i", [P, T, SIDES, TOPK], U32)
    top_f = sb("top_f", [P, T, SIDES, TOPK])
    cand = sb("cand", [P, T, NCAND])
    cand_rest = sb("cand_rest", [P, T, NCAND])
    cand_row = sb("cand_row", [P, T, NCAND])
    best = sb("best", [P, T, TOPK])
    place = sb("place", [P, T, TOPK], U32)
    onehot = sb("onehot", [P, T, TOPK, NCAND])
    gap = sb("gap", [P, T, TOPK])
    wexp = sb("wexp", [P, T, TOPK])
    wsum = sb("wsum", [P, T])
    rows = [sb(f"rows{i}", [P, T * TOPK], U32) for i in range(2)]
    wts = [sb(f"wts{i}", [P, T, TOPK]) for i in range(2)]
    qT = [sb(f"qT{i}", [P, N]) for i in range(2)]
    got = [sb(f"got{t}", [P, TOPK, 2 * D]) for t in range(T)]
    diag = [sb(f"diag{i}", [P, TOPK, P]) for i in range(2)]
    kv = sb("kv", [P, T, 2 * D])
    keyT = sb("keyT", [P, N])
    neg = sb("neg", [P, N])
    neg_max = sb("neg_max", [P, 1])
    prob = sb("prob", [P, N])
    prob_sum = sb("prob_sum", [P, 1])
    prob_inv = sb("prob_inv", [P, 1])
    probT = sb("probT", [P, N])
    headT = sb("headT", [P, P])
    acc = sb("acc", [P, T, D])
    fin = sb("fin", [P, T, D])
    front_ps = [pb("front_ps0"), pb("front_ps1")]
    comb_ps = [pb("comb_ps0"), pb("comb_ps1")]
    score_ps = pb("score_ps")
    probT_ps = pb("probT_ps")
    small_ps = pb("small_ps")
    const_ps = pb("const_ps")
    keyT_ps, headT_ps = (small_ps[:, i * P:(i + 1) * P] for i in range(2))
    proj_ps = probT_ps[:, 0:D]
    ident_ps = const_ps[:, 0:P]

    wts_loaded = sem("wts_loaded")
    x_loaded, adj_loaded, out_stored = sem("x_loaded"), sem("adj_loaded"), sem("out_stored")
    zeroed, consts = sem("zeroed"), sem("consts")
    setup_ps, setup_sb, setup_v = sem("setup_ps"), sem("setup_sb"), sem("setup_v")
    x_used, adj_cast = sem("x_used"), sem("adj_cast")
    var_ready, sd_ready = sem("var_ready"), sem("sd_ready")
    xn_ready, xnT_ready, xnT_copied = sem("xn_ready"), sem("xnT_ready"), sem("xnT_copied")
    hu_ready, hu_copied, msg_ready = sem("hu_ready"), sem("hu_copied"), sem("msg_ready")
    wq_ready, q_ready, q_copied = sem("wq_ready"), sem("q_ready"), sem("q_copied")
    sim_ready, sim_copied, sim_used = sem("sim_ready"), sem("sim_copied"), sem("sim_used")
    gap_ready, wexp_ready, rows_ready = sem("gap_ready"), sem("wexp_ready"), sem("rows_ready")
    gathered = [sem(f"gathered{t}") for t in range(T)]
    diag_ready, combined, kv_copied = sem("diag_ready"), sem("combined"), sem("kv_copied")
    keyT_ready, keyT_copied = sem("keyT_ready"), sem("keyT_copied")
    scored, neg_ready, prob_ready = sem("scored"), sem("neg_ready"), sem("prob_ready")
    probT_ready, probT_copied = sem("probT_ready"), sem("probT_copied")
    headT_ready, headT_copied = sem("headT_ready"), sem("headT_copied")
    projected, added = sem("projected"), sem("added")
    fin_ready, fin_free = sem("fin_ready"), sem("fin_free")
    chain = sem("chain")
    held = sem("held")

    def schedule(eng, setup, gnn, front, step):
        setup()
        gnn(0)
        front(0, 0, 0)
        with eng.Fori(0, B - 1) as b:
            with eng.Fori(0, H // 2 - 1) as i:
                step(b, i * 2, 0)
                step(b, i * 2 + 1, 1)
            step(b, H - 2, 0, gnn_too=True)
            step(b, H - 1, 1, last_head=True)
        with eng.Fori(0, H // 2 - 1) as i:
            step(B - 1, i * 2, 0)
            step(B - 1, i * 2 + 1, 1)
        step(B - 1, H - 2, 0)
        step(B - 1, H - 1, 1, last_head=True, last=True)

    block_ctx = nc.Block()
    block = block_ctx.__enter__()

    @block.sync
    def _(sp):
        def load_x(b):
            sp.dma_start(x_in[:, :, :], x[b].rearrange("(t p) d -> p t d", p=P)).then_inc(x_loaded, 16)

        def load_adj(b):
            sp.dma_start(adj_i[:, :, :], adj[b].rearrange("(t p) j -> p t j", p=P)).then_inc(adj_loaded, 16)

        def store(b):
            sp.dma_start(out[b].rearrange("(t p) d -> p t d", p=P), fin[:, :, :]).then_inc(out_stored, 16)

        load_x(0)
        load_adj(0)
        sp.dma_start(w_hu[:, 0:D], w_msg).then_inc(wts_loaded, 16)
        sp.dma_start(w_hu[:, D:2 * D], w_upd).then_inc(wts_loaded, 16)
        sp.dma_start(bias_all[:, :], bias.partition_broadcast(P)).then_inc(wts_loaded, 16)
        sp.dma_start(wqpk_sb[:, :], wqpk_t).then_inc(wts_loaded, 16)
        sp.dma_start(keys_sb[:, :], keys_t).then_inc(wts_loaded, 16)
        sp.dma_start(wq_sb[:, :], wq).then_inc(wts_loaded, 16)
        sp.dma_start(wo_sb[:, :, :], wo.rearrange("(h d) n -> d h n", d=D)).then_inc(wts_loaded, 16)
        sp.sem_inc(fin_free, 1)
        with sp.Fori(0, B - 1) as b:
            sp.wait_ge(x_used, b + 1)
            load_x(b + 1)
            sp.wait_ge(adj_cast, b + 1)
            load_adj(b + 1)
            sp.wait_ge(fin_ready, (b + 1) * T)
            store(b)
            sp.wait_ge(out_stored, (b + 1) * 16)
            sp.sem_inc(fin_free, 1)
        sp.wait_ge(fin_ready, B * T)
        store(B - 1)
        sp.wait_ge(out_stored, B * 16)

    @block.gpsimd
    def _(pool):
        pool.memset(ident[:, :], 0.0).then_inc(zeroed, 1)
        pool.memset(mask[:, :], 0.0).then_inc(zeroed, 1)
        pool.iota(iota_i[:, :], pattern=[[1, NCAND]], base=0, channel_multiplier=0).then_inc(consts, 1)
        pool.wait_ge(zeroed, 2)
        pool.affine_select(out=ident[:, :], in_=ident[:, :], compare_op=ALU.not_equal, fill=1.0, base=0,
                           pattern=[[-1, P]], channel_multiplier=1).then_inc(consts, 1)
        pool.affine_select(out=mask[:, :], in_=mask[:, :], compare_op=ALU.is_ge, fill=LOWEST, base=N - P,
                           pattern=[[-1, N]], channel_multiplier=1).then_inc(consts, 1)

        def step(s, par, first=False):
            pool.wait_ge(rows_ready, s + 1)
            pool.sem_inc(held, 1)
            for t in range(T):
                if not first:
                    pool.wait_ge(combined, s * T + (t + 1 - T))
                    pool.sem_inc(held, 1)
                for k in range(TOPK):
                    pool.indirect_dma_start(
                        out=got[t][:, k, :], out_offset=None, in_=table,
                        in_offset=bass.IndirectOffsetOnAxis(ap=rows[par][:, t * TOPK + k:t * TOPK + k + 1], axis=0),
                    ).then_inc(gathered[t], 16)

        step(0, 0, first=True)
        with pool.Fori(0, (STEPS - 2) // 2) as i:
            step(i * 2 + 1, 1)
            step(i * 2 + 2, 0)
        step(STEPS - 1, 1)

    @block.tensor
    def _(pe):
        def setup():
            pe.wait_ge(wts_loaded, 7 * 16)
            pe.wait_ge(consts, 3)
            for g in range(SIDES * H // 4):
                if g >= 2:
                    pe.wait_ge(setup_sb, g - 1)
                for j in range(4):
                    c = (g * 4 + j) * P
                    last = pe.matmul(front_ps[g % 2][:, j * P:(j + 1) * P], wqpk_sb[:, c:c + P],
                                     keys_sb[:, c:c + P], start=True, stop=True)
                last.then_inc(setup_ps, 1)
            pe.wait_ge(setup_sb, SIDES * H // 4)
            pe.wait_ge(setup_v, 1)

        def transpose_xn(n):
            pe.wait_ge(xn_ready, n + 1)
            for t in range(T):
                last = pe.transpose(front_ps[0][:, t * P:(t + 1) * P], xn[:, t, :], ident[:, :])
            last.then_inc(xnT_ready, 1)

        def gnn(b):
            if not isinstance(b, int):
                pe.wait_ge(q_copied, b * H)
                pe.wait_ge(sim_copied, b * H * 2)
            transpose_xn(b * 2)
            for i in range(2):
                if i == 0:
                    pe.wait_ge(xnT_copied, b * 2 + 1)
                for t in (2 * i, 2 * i + 1):
                    last = pe.matmul(front_ps[1 - i][:, (t % 2) * 2 * D:(t % 2 + 1) * 2 * D],
                                     xnT[:, t * P:(t + 1) * P], w_hu[:, :], start=True, stop=True)
                last.then_inc(hu_ready, 1)
            pe.wait_ge(adj_cast, b + 1)
            for i in range(2):
                pe.wait_ge(hu_copied, b * 2 + 2)
                for t in (2 * i, 2 * i + 1):
                    for j in range(T):
                        last = pe.matmul(front_ps[1 - i][:, (t % 2) * 2 * D:(t % 2) * 2 * D + D + 1],
                                         adj_f[:, j, t * P:(t + 1) * P], hu[:, j, 0:D + 1],
                                         start=(j == 0), stop=(j == T - 1))
                last.then_inc(msg_ready, 1)
            transpose_xn(b * 2 + 1)

        def front(b, h, par, first_head=False):
            f = b * H + h
            if first_head:
                pe.wait_ge(xnT_copied, b * 2 + 2)
            for i in range(2):
                if i == 0:
                    pe.wait_ge(q_copied, f)
                else:
                    pe.wait_ge(sim_copied, f * 2)
                for t in (2 * i, 2 * i + 1):
                    last = pe.matmul(front_ps[i][:, (t % 2) * 256:(t % 2 + 1) * 256], x2nT[:, t * P:(t + 1) * P],
                                     w_sim[:, bass.ds(h * 256, 256)], start=True, stop=True)
                last.then_inc(sim_ready, 1)
            pe.wait_ge(wq_ready, f + 1)
            pe.wait_ge(sim_copied, f * 2 + 1)
            pe.matmul(front_ps[0][:, :], wq_head[:, :], x2nT[:, :], start=True, stop=True).then_inc(q_ready, 1)

        def step(b, h, par, gnn_too=False, last_head=False, last=False):
            s = b * H + h
            if last_head and not last:
                front(b + 1, 0, 1 - par, first_head=True)
            elif not last:
                front(b, h + 1, 1 - par)

            def combine(t, k0, k1):
                if k0 == 0:
                    pe.wait_ge(gathered[t], s * (TOPK * 16) + TOPK * 16)
                    pe.wait_ge(diag_ready, s * T + t + 1)
                for k in range(k0, k1):
                    last = pe.matmul(comb_ps[t % 2][:, 0:2 * D], diag[t % 2][:, k, :], got[t][:, k, :],
                                     start=(k == 0), stop=(k == TOPK - 1))
                if k1 == TOPK:
                    last.then_inc(combined, 1)

            def key_transpose(t):
                pe.wait_ge(kv_copied, s * T + t + 1)
                pe.transpose(keyT_ps, kv[:, t, 0:D], ident[:, :]).then_inc(keyT_ready, 1)

            def scores(t):
                if t == 0:
                    pe.wait_ge(q_copied, s + 1)
                pe.wait_ge(keyT_copied, s * T + t + 1)
                pe.matmul(score_ps[:, 0:(t + 1) * P], qT[par][:, t * P:(t + 1) * P], keyT[:, 0:(t + 1) * P],
                          start=True, stop=True).then_inc(scored, 1)

            def prob_transpose(t):
                pe.wait_ge(prob_ready, s * T + t + 1)
                if t:
                    pe.wait_ge(added, s * T + t)
                for j in range(t + 1):
                    last = pe.transpose(probT_ps[:, j * P:(j + 1) * P], prob[:, j * P:(j + 1) * P], ident[:, :])
                last.then_inc(probT_ready, 1)

            def values(t):
                pe.wait_ge(probT_copied, s * T + t + 1)
                for j in range(t + 1):
                    last = pe.matmul(headT_ps, kv[:, j, D:2 * D], probT[:, j * P:(j + 1) * P],
                                     start=(j == 0), stop=(j == t))
                last.then_inc(headT_ready, 1)

            def project(t):
                pe.wait_ge(headT_copied, s * T + t + 1)
                pe.matmul(proj_ps, headT[:, :], wo_sb[:, bass.ds(h, 1), :].rearrange("p a n -> p (a n)"),
                          start=True, stop=True).then_inc(projected, 1)

            stages = (key_transpose, scores, prob_transpose, values, project)
            cuts = (0, 3, 5, 10, 13, TOPK)
            combine(0, 0, TOPK)
            for t in range(1, T):
                for stage, k0, k1 in zip(stages, cuts, cuts[1:]):
                    combine(t, k0, k1)
                    stage(t - 1)
                if t == 2 and gnn_too:
                    gnn(b + 1)
            for stage in stages:
                stage(T - 1)

        def first_front(b, h, par):
            front(b, h, par, first_head=True)

        schedule(pe, setup, gnn, first_front, step)

    @block.scalar
    def _(act):
        def copy(dst, src, scale=1.0):
            return act.activation(dst, src, ACT.Copy, scale=scale)

        def setup():
            for g in range(SIDES * H // 4):
                act.wait_ge(setup_ps, g + 1)
                copy(w_sim[:, g * 512:(g + 1) * 512], front_ps[g % 2][:, :]).then_inc(setup_sb, 1)

        def root(n):
            act.wait_ge(var_ready, n + 1)
            act.activation(sd[:, :], var[:, :], ACT.Sqrt).then_inc(sd_ready, 1)

        def gnn(b):
            act.wait_ge(adj_loaded, b * 16 + 16)
            copy(adj_f[:, :, :], adj_i[:, :, :]).then_inc(adj_cast, 1)
            root(b * 2)
            act.wait_ge(xnT_ready, b * 2 + 1)
            copy(xnT[:, :], front_ps[0][:, :]).then_inc(xnT_copied, 1)
            for i in range(2):
                act.wait_ge(hu_ready, b * 2 + i + 1)
                ps = front_ps[1 - i][:, :].rearrange("p (t c) -> p t c", t=2)
                copy(hu[:, 2 * i:2 * i + 2, 0:D], ps[:, :, 0:D])
                copy(hu[:, 2 * i:2 * i + 2, D + 1:], ps[:, :, D:2 * D]).then_inc(hu_copied, 1)
            root(b * 2 + 1)
            act.wait_ge(xnT_ready, b * 2 + 2)
            copy(x2nT[:, :], front_ps[0][:, :]).then_inc(xnT_copied, 1)

        def front(b, h, par, first=False):
            f = b * H + h
            act.wait_ge(q_ready, f)
            act.sem_inc(held, 1)
            copy(wq_head[:, :], wq_sb[:, bass.ds(h * D, D)]).then_inc(wq_ready, 1)
            for i in range(2):
                act.wait_ge(sim_ready, f * 2 + i + 1)
                if not first:
                    act.wait_ge(sim_used, f * 2 + (i - 1))
                copy(sim[:, 2 * i:2 * i + 2, :], front_ps[i][:, :]).then_inc(sim_copied, 1)
            act.wait_ge(q_ready, f + 1)
            copy(qT[par][:, :], front_ps[0][:, :], scale=SCALE).then_inc(q_copied, 1)

        def weights(f):
            act.wait_ge(gap_ready, f + 1)
            act.activation(wexp[:, :, :], gap[:, :, :], ACT.Exp).then_inc(wexp_ready, 1)

        def first_front(b, h, par):
            front(b, h, par, first=True)
            weights(b * H + h)

        def step(b, h, par, gnn_too=False, last_head=False, last=False):
            s = b * H + h
            if last_head and not last:
                front(b + 1, 0, 1 - par)
            elif not last:
                front(b, h + 1, 1 - par)

            def take_kv(t):
                act.wait_ge(combined, s * T + t + 1)
                copy(kv[:, t, :], comb_ps[t % 2][:, 0:2 * D]).then_inc(kv_copied, 1)

            def take_keyT(t):
                act.wait_ge(keyT_ready, s * T + t + 1)
                copy(keyT[:, t * P:(t + 1) * P], keyT_ps).then_inc(keyT_copied, 1)

            def exponent(t):
                act.wait_ge(neg_ready, s * T + t + 1)
                act.activation(prob[:, 0:(t + 1) * P], neg[:, 0:(t + 1) * P], ACT.Exp, bias=neg_max[:, :],
                               scale=-1.0, accum_out=prob_sum[:, :]).then_inc(prob_ready, 1)

            def take_probT(t):
                act.wait_ge(probT_ready, s * T + t + 1)
                copy(probT[:, 0:(t + 1) * P], probT_ps[:, 0:(t + 1) * P]).then_inc(probT_copied, 1)

            def take_headT(t):
                act.wait_ge(headT_ready, s * T + t + 1)
                copy(headT[:, :], headT_ps).then_inc(headT_copied, 1)

            def attend(t):
                take_keyT(t)
                exponent(t)
                take_probT(t)
                take_headT(t)

            for t in range(T):
                if t:
                    attend(t - 1)
                take_kv(t)
                if t == 1 and not last:
                    weights(s + 1)
                if t == 2 and gnn_too:
                    gnn(b + 1)
            attend(T - 1)

        schedule(act, setup, gnn, first_front, step)

    @block.vector
    def _(dve):
        count = [0]

        def link(instruction):
            instruction.then_inc(chain, 1)
            count[0] += 1
            return count[0]

        def after(n):
            dve.wait_ge(chain, n)

        def restart():
            after(count[0])
            dve.sem_clear(chain)
            count[0] = 0

        def setup():
            dve.wait_ge(consts, 3)
            dve.tensor_copy(ident_ps, ident[:, :])
            dve.tensor_copy(iota_f[:, :], iota_i[:, :])
            for h in range(H):
                dve.memset(head_row[:, h:h + 1], float(h * ROWS))
            n = link(dve.memset(hu[:, :, D:D + 1], 1.0))
            after(n)
            dve.sem_inc(setup_v, 1)
            restart()

        def layernorm(src, n):
            for t in range(T):
                a = link(dve.bn_stats(stats[:, t, :], src[:, t, :]))
            for t in range(T):
                after(a - T + 1 + t)
                c = link(dve.bn_aggr(meanvar[:, t, :], stats[:, t, :]))
            after(c)
            dve.tensor_scalar(var[:, :], meanvar[:, :, 1], EPS, None, ALU.add).then_inc(var_ready, 1)
            dve.wait_ge(sd_ready, n + 1)
            after(link(dve.reciprocal(rstd[:, :], sd[:, :])))
            after(link(dve.tensor_tensor(rstd2[:, :], rstd[:, :], rstd[:, :], ALU.mult)))
            after(link(dve.tensor_tensor(rstd2[:, :], rstd2[:, :], var[:, :], ALU.mult)))
            after(link(dve.tensor_scalar(rstd2[:, :], rstd2[:, :], -0.5, 1.5, ALU.mult, ALU.add)))
            after(link(dve.tensor_tensor(rstd[:, :], rstd[:, :], rstd2[:, :], ALU.mult)))
            for t in range(T):
                a = link(dve.tensor_scalar(xn[:, t, :], src[:, t, :], meanvar[:, t, 0:1], rstd[:, t:t + 1],
                                           ALU.subtract, ALU.mult))
            after(a)
            dve.sem_inc(xn_ready, 1)

        def gnn(b):
            restart()
            dve.wait_ge(x_loaded, b * 16 + 16)
            dve.sem_inc(held, 1)
            layernorm(x_in, b * 2)
            for i in range(2):
                dve.wait_ge(msg_ready, b * 2 + i + 1)
                ps = front_ps[1 - i][:, :].rearrange("p (t c) -> p t c", t=2)
                d, g = deg[:, 2 * i:2 * i + 2], degpos[:, 2 * i:2 * i + 2]
                a = link(dve.tensor_scalar(d, ps[:, :, D], 1.0, None, ALU.max))
                c = link(dve.tensor_scalar(g, ps[:, :, D], 0.0, None, ALU.is_gt))
                after(a)
                after(link(dve.reciprocal(d, d)))
                after(link(dve.tensor_tensor(d, d, g, ALU.mult)))
                for t in (2 * i, 2 * i + 1):
                    a = link(dve.scalar_tensor_tensor(upd[:, t, :], ps[:, t % 2, 0:D], deg[:, t:t + 1],
                                                      hu[:, t, D + 1:], ALU.mult, ALU.add))
            after(a)
            after(link(dve.tensor_tensor(upd[:, :, :], upd[:, :, :],
                                         bias_all[:, :].unsqueeze(1).broadcast_to([P, T, D]), ALU.add)))
            after(link(dve.scalar_tensor_tensor(x2[:, :, :], upd[:, :, :], 0.0, x_in[:, :, :], ALU.max, ALU.add)))
            dve.sem_inc(x_used, 1)
            if isinstance(b, int):
                link(dve.tensor_copy(acc[:, :, :], x2[:, :, :]))
            layernorm(x2, b * 2 + 1)

        def rank(f, i):
            dve.wait_ge(sim_copied, f * 2 + i + 1)
            dve.sem_inc(held, 1)
            lanes = [(2 * i + u, p, 2 * u + p) for u in range(2) for p in range(SIDES)]
            full = [sim[:, t, p * NKEYS:(p + 1) * NKEYS] for t, p, _ in lanes]
            rest = [sim_rest[:, r, :] for _, _, r in lanes]
            for n in range(5):
                for (t, p, r), src, left in zip(lanes, full, rest):
                    v, ix = top_v[:, t, p, :], top_i[:, t, p, :]
                    if n:
                        after(count[0] - len(lanes) + 1)
                    if n == 0:
                        link(dve.max(v[:, 0:8], src))
                    if n == 1:
                        link(dve.max_index(ix[:, 0:8], v[:, 0:8], src))
                    if n == 2:
                        link(dve.match_replace(left, v[:, 0:8], src, LOWEST))
                    if n == 3:
                        link(dve.max(v[:, 8:16], left))
                    if n == 4:
                        link(dve.max_index(ix[:, 8:16], v[:, 8:16], left))
            after(count[0])
            dve.sem_inc(sim_used, 1)

        def choose(f, h, par):
            a = link(dve.tensor_copy(top_f[:, :, 0, :], top_i[:, :, 0, :]))
            c = link(dve.tensor_scalar(top_f[:, :, 1, :], top_i[:, :, 1, :], float(NKEYS),
                                       head_row[:, bass.ds(h, 1)], ALU.mult, ALU.add))
            for dst, src in ((cand, top_v), (cand_row, top_f)):
                for i, n in GROUPS:
                    w = RUN[i]
                    if src is top_f:
                        after(c)
                    o = dst[:, :, START[i]:START[i] + n * w].rearrange("p t (a w) -> p t a w", a=n)
                    link(dve.tensor_tensor(o, src[:, :, 0, i:i + n].unsqueeze(3).broadcast_to([P, T, n, w]),
                                           src[:, :, 1, 0:w].unsqueeze(2).broadcast_to([P, T, n, w]), ALU.add))
            after(count[0])
            for n in range(5):
                for t in range(T):
                    if n:
                        after(count[0] - T + 1)
                    v, ix = best[:, t, :], place[:, t, :]
                    if n == 0:
                        link(dve.max(v[:, 0:8], cand[:, t, :]))
                    if n == 1:
                        link(dve.max_index(ix[:, 0:8], v[:, 0:8], cand[:, t, :]))
                    if n == 2:
                        link(dve.match_replace(cand_rest[:, t, :], v[:, 0:8], cand[:, t, :], LOWEST))
                    if n == 3:
                        link(dve.max(v[:, 8:16], cand_rest[:, t, :]))
                    if n == 4:
                        link(dve.max_index(ix[:, 8:16], v[:, 8:16], cand_rest[:, t, :]))
                if n == 3:
                    after(count[0])
                    dve.tensor_tensor(gap[:, :, :], best[:, :, :], best[:, :, 0:1].broadcast_to([P, T, TOPK]),
                                      ALU.subtract).then_inc(gap_ready, 1)
            after(count[0])
            flat = onehot[:, :, :, :].rearrange("p t k c -> p (t k) c")
            n = T * TOPK
            after(link(dve.tensor_tensor(
                flat, place[:, :, :].rearrange("p t k -> p (t k)").unsqueeze(2).broadcast_to([P, n, NCAND]),
                iota_f[:, :].unsqueeze(1).broadcast_to([P, n, NCAND]), ALU.is_equal)))
            after(link(dve.tensor_tensor(onehot[:, :, :, :], onehot[:, :, :, :],
                                         cand_row[:, :, :].unsqueeze(2).broadcast_to([P, T, TOPK, NCAND]), ALU.mult)))
            with nc.allow_low_precision(reason="the sum of one row number and zeros"):
                dve.tensor_reduce(rows[par][:, :], flat, AX.X, ALU.add).then_inc(rows_ready, 1)
            dve.wait_ge(wexp_ready, f + 1)
            after(link(dve.tensor_reduce(wsum[:, :], wexp[:, :, :], AX.X, ALU.add)))
            after(link(dve.reciprocal(wsum[:, :], wsum[:, :])))
            after(link(dve.tensor_tensor(wts[par][:, :, :], wexp[:, :, :],
                                         wsum[:, :].unsqueeze(2).broadcast_to([P, T, TOPK]), ALU.mult)))

        def first_front(b, h, par):
            rank(b * H + h, 0)
            rank(b * H + h, 1)
            choose(b * H + h, h, par)
            restart()

        def step(b, h, par, gnn_too=False, last_head=False, last=False):
            s = b * H + h

            def weigh(t):
                if t >= 2:
                    dve.wait_ge(combined, s * T + t - 1)
                dve.tensor_tensor(diag[t % 2][:, :, :], ident_ps.unsqueeze(1).broadcast_to([P, TOPK, P]),
                                  wts[par][:, t, :].unsqueeze(2).broadcast_to([P, TOPK, P]),
                                  ALU.mult).then_inc(diag_ready, 1)

            def negate(t):
                dve.wait_ge(scored, s * T + t + 1)
                dve.sem_inc(held, 1)
                n = (t + 1) * P
                dve.tensor_tensor_reduce(out=neg[:, 0:n], in0=score_ps[:, 0:n], in1=mask[:, N - n:N], scale=-1.0,
                                         scalar=-LOWEST, op0=ALU.add, op1=ALU.min,
                                         accum_out=neg_max[:, :]).then_inc(neg_ready, 1)

            def add(t):
                dve.wait_ge(prob_ready, s * T + t + 1)
                a = link(dve.reciprocal(prob_inv[:, :], prob_sum[:, :]))
                dve.wait_ge(projected, s * T + t + 1)
                after(a)
                if last_head:
                    if t == 0:
                        dve.wait_ge(fin_free, b + 1)
                    a = link(dve.scalar_tensor_tensor(fin[:, t, :], proj_ps, prob_inv[:, :], acc[:, t, :],
                                                      ALU.mult, ALU.add))
                    after(a)
                    dve.sem_inc(fin_ready, 1)
                    dve.sem_inc(added, 1)
                    if not last:
                        link(dve.tensor_copy(acc[:, t, :], x2[:, t, :]))
                else:
                    a = link(dve.scalar_tensor_tensor(acc[:, t, :], proj_ps, prob_inv[:, :], acc[:, t, :],
                                                      ALU.mult, ALU.add))
                    after(a)
                    dve.sem_inc(added, 1)

            weigh(0)
            weigh(1)
            if not last:
                rank(s + 1, 0)
            negate(0)
            add(0)
            weigh(2)
            if not last:
                rank(s + 1, 1)
                choose(s + 1, 0 if last_head else h + 1, 1 - par)
            negate(1)
            add(1)
            if gnn_too:
                gnn(b + 1)
            weigh(3)
            negate(2)
            add(2)
            negate(3)
            add(3)
            restart()

        schedule(dve, setup, gnn, first_front, step)

    block_ctx.__exit__(None, None, None)


def kernel(x, adj, L0_gnn_W_msg, L0_gnn_W_upd, L0_gnn_bias, L0_ffn_Wq_pk, L0_ffn_pk_keys, L0_ffn_Wq,
           L0_ffn_keys_table, L0_ffn_values_table, L0_ffn_Wo):
    import numpy as np
    import concourse.bacc as bacc
    from concourse.bass_utils import run_bass_kernel_spmd as run

    c = np.ascontiguousarray
    wqpk = np.asarray(L0_ffn_Wq_pk).reshape(D, SIDES, H, DKEY)
    keys = np.asarray(L0_ffn_pk_keys)
    arrays = {
        "x": c(x), "adj": c(adj), "w_msg": c(L0_gnn_W_msg), "w_upd": c(L0_gnn_W_upd), "bias": c(L0_gnn_bias),
        "wqpk_t": c(wqpk.transpose(3, 2, 1, 0).reshape(DKEY, H * SIDES * D)),
        "keys_t": c(keys.transpose(3, 2, 0, 1).reshape(DKEY, H * SIDES * NKEYS)),
        "wq": c(L0_ffn_Wq),
        "table": c(np.concatenate([np.asarray(L0_ffn_keys_table), np.asarray(L0_ffn_values_table)], axis=1)),
        "wo": c(L0_ffn_Wo),
    }
    nc = bacc.Bacc("TRN2", target_bir_lowering=False, num_devices=1)
    args = [nc.dram_tensor(f"in_{n}", a.shape, mybir.dt.from_np(a.dtype), kind="ExternalInput").ap()
            for n, a in arrays.items()]
    out = nc.dram_tensor("out", (B, N, D), F32, kind="ExternalOutput").ap()
    program(nc, *args, out)
    r = run(nc, [{f"in_{n}": a for n, a in arrays.items()}], core_ids=[0])
    return np.asarray(r.results[0]["out"])
```

```python
from concourse import bass, mybir
from concourse.alu_op_type import AluOpType as ALU

F32 = mybir.dt.float32
U32 = mybir.dt.uint32
I32 = mybir.dt.int32
ACT = mybir.ActivationFunctionType
AX = mybir.AxisListType

P = 128
B, N, D = 16, 512, 128
T = N // P
H = 8
SIDES, NKEYS, DKEY = 2, 128, 64
TOPK = 16
ROWS = NKEYS * NKEYS
STEPS = B * H
QUARTERS = 4
RUN = [TOPK // (i + 1) for i in range(TOPK)]
START = [sum(RUN[:i]) for i in range(TOPK)]
NCAND = sum(RUN)
GROUPS = []
for _i in range(TOPK):
    if GROUPS and RUN[GROUPS[-1][0]] == RUN[_i]:
        GROUPS[-1][1] += 1
    else:
        GROUPS.append([_i, 1])
PAIRS = [(0, 2), (2, 2)]
FIRST_TILES = [(0, 1), (1, 1), (2, 2)]
LOWEST = -3.4e38
EPS = 1e-5
SCALE = float(D) ** -0.5


def program(nc, x, adj, w_msg, w_upd, bias, wqpk_t, keys_t, wq, table, wo, out):
    def sb(name, shape, dt=F32):
        return nc.alloc_sbuf_tensor(name, shape, dt)

    def pb(name):
        return nc.alloc_psum_tensor(name, [P, 512], F32)

    sem = nc.alloc_semaphore

    w_hu = sb("w_hu", [P, 2 * D])
    bias_all = sb("bias_all", [P, D])
    wqpk_sb = sb("wqpk_sb", [DKEY, SIDES * H * D])
    keys_sb = sb("keys_sb", [DKEY, SIDES * H * NKEYS])
    w_sim = sb("w_sim", [P, H * SIDES * NKEYS])
    wq_sb = sb("wq_sb", [P, H * D])
    wq_head = sb("wq_head", [P, D])
    wo_sb = sb("wo_sb", [P, H, D])
    ident = sb("ident", [P, P])
    mask = sb("mask", [P, N])
    iota_i = sb("iota_i", [P, NCAND], I32)
    head_row = sb("head_row", [P, H])
    x_in = sb("x_in", [P, T, D])
    adj_i = sb("adj_i", [P, T, N], I32)
    adj_f = sb("adj_f", [P, T, N])
    stats = sb("stats", [P, T, 6])
    meanvar = sb("meanvar", [P, T, 2])
    var = sb("var", [P, T])
    sd = sb("sd", [P, T])
    rstd = sb("rstd", [P, T])
    rstd2 = sb("rstd2", [P, T])
    xn = sb("xn", [P, T, D])
    xnT = sb("xnT", [P, N])
    hu = sb("hu", [P, T, 2 * D + 1])
    deg = sb("deg", [P, T])
    degpos = sb("degpos", [P, T])
    upd = sb("upd", [P, T, D])
    x2 = sb("x2", [P, T, D])
    x2nT = sb("x2nT", [P, N])
    sim = sb("sim", [P, T, SIDES * NKEYS])
    sim_rest = sb("sim_rest", [P, 2 * SIDES, NKEYS])
    top_v = sb("top_v", [P, T, SIDES, TOPK])
    top_i = sb("top_i", [P, T, SIDES, TOPK], U32)
    top_f = sb("top_f", [P, T, SIDES, TOPK])
    cand = sb("cand", [P, T, NCAND])
    cand_rest = sb("cand_rest", [P, T, NCAND])
    best = sb("best", [P, T, TOPK])
    place = sb("place", [P, T, TOPK], U32)
    onehot = sb("onehot", [P, 2, TOPK, NCAND])
    gap = sb("gap", [P, T, TOPK])
    wexp = sb("wexp", [P, T, TOPK])
    wsum = sb("wsum", [P, T])
    rows = [sb(f"rows{i}", [P, T * TOPK], U32) for i in range(2)]
    wts = [sb(f"wts{i}", [P, T, TOPK]) for i in range(2)]
    qT = [sb(f"qT{i}", [P, N]) for i in range(2)]
    got = [sb(f"got{t}", [P, TOPK, 2 * D]) for t in range(T)]
    diag = [sb(f"diag{i}", [P, TOPK, P]) for i in range(2)]
    kv = sb("kv", [P, T, 2 * D])
    keyT = sb("keyT", [P, N])
    neg = sb("neg", [P, N])
    neg_max = sb("neg_max", [P, 1])
    prob = sb("prob", [P, N])
    prob_sum = sb("prob_sum", [P, 1])
    prob_inv = sb("prob_inv", [P, 1])
    probT = sb("probT", [P, N])
    headT = sb("headT", [P, P])
    acc = sb("acc", [P, T, D])
    fin = sb("fin", [P, T, D])
    front_ps = [pb("front_ps0"), pb("front_ps1")]
    comb_ps = [pb("comb_ps0"), pb("comb_ps1")]
    score_ps = pb("score_ps")
    probT_ps = pb("probT_ps")
    small_ps = pb("small_ps")
    const_ps = pb("const_ps")
    keyT_ps, headT_ps = (small_ps[:, i * P:(i + 1) * P] for i in range(2))
    proj_ps = probT_ps[:, 0:D]
    ident_ps = const_ps[:, 0:P]
    iota_ps = const_ps[:, P:P + NCAND]
    cand_row = const_ps[:, 256:256 + T * NCAND].rearrange("p (t c) -> p t c", t=T)
    fold_ps = [score_ps, probT_ps]

    gnn_loaded, keys_loaded, heads_loaded = sem("gnn_loaded"), sem("keys_loaded"), sem("heads_loaded")
    x_loaded, adj_loaded, out_stored = sem("x_loaded"), sem("adj_loaded"), sem("out_stored")
    zeroed, consts = sem("zeroed"), sem("consts")
    fold_ready, fold_copied, ones_ready = sem("fold_ready"), sem("fold_copied"), sem("ones_ready")
    x_used, adj_cast = sem("x_used"), sem("adj_cast")
    var_ready, sd_ready = sem("var_ready"), sem("sd_ready")
    xn_ready, xnT_ready, xnT_copied = sem("xn_ready"), sem("xnT_ready"), sem("xnT_copied")
    hu_ready, hu_copied, msg_ready = sem("hu_ready"), sem("hu_copied"), sem("msg_ready")
    wq_ready, q_ready, q_copied = sem("wq_ready"), sem("q_ready"), sem("q_copied")
    sim_ready, sim_copied, sim_used = sem("sim_ready"), sem("sim_copied"), sem("sim_used")
    gap_ready, wexp_ready, rows_ready = sem("gap_ready"), sem("wexp_ready"), sem("rows_ready")
    gathered = [sem(f"gathered{t}") for t in range(T)]
    gathered_end = [sem(f"gathered_end{i}") for i in range(QUARTERS)]
    diag_ready, combined, kv_copied = sem("diag_ready"), sem("combined"), sem("kv_copied")
    keyT_ready, keyT_copied = sem("keyT_ready"), sem("keyT_copied")
    scored, neg_ready, prob_ready = sem("scored"), sem("neg_ready"), sem("prob_ready")
    probT_ready, probT_copied = sem("probT_ready"), sem("probT_copied")
    headT_ready, headT_copied = sem("headT_ready"), sem("headT_copied")
    projected, added = sem("projected"), sem("added")
    fin_ready, fin_free = sem("fin_ready"), sem("fin_free")
    chain = sem("chain")
    held = sem("held")

    def schedule(eng, first, step):
        first()
        with eng.Fori(0, B - 1) as b:
            with eng.Fori(0, H // 2 - 1) as i:
                step(b, i * 2, 0)
                step(b, i * 2 + 1, 1)
            step(b, H - 2, 0, gnn_too=True)
            step(b, H - 1, 1, last_head=True)
        with eng.Fori(0, H // 2 - 1) as i:
            step(B - 1, i * 2, 0)
            step(B - 1, i * 2 + 1, 1)
        step(B - 1, H - 2, 0)
        step(B - 1, H - 1, 1, last_head=True, last=True)

    block_ctx = nc.Block()
    block = block_ctx.__enter__()

    @block.sync
    def _(sp):
        def load_x(b):
            sp.dma_start(x_in[:, :, :], x[b].rearrange("(t p) d -> p t d", p=P)).then_inc(x_loaded, 16)

        def load_adj(b):
            sp.dma_start(adj_i[:, :, :], adj[b].rearrange("(t p) j -> p t j", p=P)).then_inc(adj_loaded, 16)

        def store(b):
            sp.dma_start(out[b].rearrange("(t p) d -> p t d", p=P), fin[:, :, :]).then_inc(out_stored, 16)

        load_x(0)
        sp.dma_start(w_hu[:, 0:D], w_msg).then_inc(gnn_loaded, 16)
        sp.dma_start(w_hu[:, D:2 * D], w_upd).then_inc(gnn_loaded, 16)
        sp.dma_start(bias_all[:, :], bias.partition_broadcast(P)).then_inc(gnn_loaded, 16)
        load_adj(0)
        sp.dma_start(wqpk_sb[:, :], wqpk_t).then_inc(keys_loaded, 16)
        sp.dma_start(keys_sb[:, :], keys_t).then_inc(keys_loaded, 16)
        sp.dma_start(wq_sb[:, :], wq).then_inc(heads_loaded, 16)
        sp.dma_start(wo_sb[:, :, :], wo.rearrange("(h d) n -> d h n", d=D)).then_inc(heads_loaded, 16)
        sp.sem_inc(fin_free, 1)
        with sp.Fori(0, B - 1) as b:
            sp.wait_ge(x_used, b + 1)
            load_x(b + 1)
            sp.wait_ge(adj_cast, b + 1)
            load_adj(b + 1)
            sp.wait_ge(fin_ready, (b + 1) * T)
            store(b)
            sp.wait_ge(out_stored, (b + 1) * 16)
            sp.sem_inc(fin_free, 1)
        sp.wait_ge(fin_ready, B * T)
        store(B - 1)
        sp.wait_ge(out_stored, B * 16)

    @block.gpsimd
    def _(pool):
        pool.memset(ident[:, :], 0.0).then_inc(zeroed, 1)
        pool.memset(mask[:, :], 0.0).then_inc(zeroed, 1)
        pool.iota(iota_i[:, :], pattern=[[1, NCAND]], base=0, channel_multiplier=0).then_inc(consts, 1)
        pool.wait_ge(zeroed, 2)
        pool.affine_select(out=ident[:, :], in_=ident[:, :], compare_op=ALU.not_equal, fill=1.0, base=0,
                           pattern=[[-1, P]], channel_multiplier=1).then_inc(consts, 1)
        pool.affine_select(out=mask[:, :], in_=mask[:, :], compare_op=ALU.is_ge, fill=LOWEST, base=N - P,
                           pattern=[[-1, N]], channel_multiplier=1).then_inc(consts, 1)

        def step(s, par, first=False, last=False):
            for t in range(T):
                pool.wait_ge(rows_ready, s * T + t + 1)
                pool.sem_inc(held, 1)
                if not first:
                    pool.wait_ge(combined, s * T + (t + 1 - T))
                    pool.sem_inc(held, 1)
                for k in range(TOPK):
                    pool.indirect_dma_start(
                        out=got[t][:, k, :], out_offset=None, in_=table,
                        in_offset=bass.IndirectOffsetOnAxis(ap=rows[par][:, t * TOPK + k:t * TOPK + k + 1], axis=0),
                    ).then_inc(gathered_end[k * QUARTERS // TOPK] if last and t == T - 1 else gathered[t], 16)

        step(0, 0, first=True)
        with pool.Fori(0, (STEPS - 2) // 2) as i:
            step(i * 2 + 1, 1)
            step(i * 2 + 2, 0)
        step(STEPS - 1, 1, last=True)

    @block.tensor
    def _(pe):
        def fold():
            pe.wait_ge(keys_loaded, 2 * 16)
            for g in range(SIDES * H // 4):
                if g >= 2:
                    pe.wait_ge(fold_copied, g - 1)
                for j in range(4):
                    c = (g * 4 + j) * P
                    last = pe.matmul(fold_ps[g % 2][:, j * P:(j + 1) * P], wqpk_sb[:, c:c + P],
                                     keys_sb[:, c:c + P], start=True, stop=True)
                last.then_inc(fold_ready, 1)
            pe.wait_ge(fold_copied, SIDES * H // 4)

        def transpose_xn(n):
            pe.wait_ge(xn_ready, n + 1)
            for t in range(T):
                last = pe.transpose(front_ps[0][:, t * P:(t + 1) * P], xn[:, t, :], ident[:, :])
            last.then_inc(xnT_ready, 1)

        def gnn_hu(b):
            transpose_xn(b * 2)
            pe.wait_ge(xnT_copied, b * 2 + 1)
            for i in range(2):
                for t in (2 * i, 2 * i + 1):
                    last = pe.matmul(front_ps[1 - i][:, (t % 2) * 2 * D:(t % 2 + 1) * 2 * D],
                                     xnT[:, t * P:(t + 1) * P], w_hu[:, :], start=True, stop=True)
                last.then_inc(hu_ready, 1)

        def gnn_msg(b):
            pe.wait_ge(adj_cast, b + 1)
            pe.wait_ge(hu_copied, b * 2 + 2)
            for i in range(2):
                for t in (2 * i, 2 * i + 1):
                    for j in range(T):
                        last = pe.matmul(front_ps[1 - i][:, (t % 2) * 2 * D:(t % 2) * 2 * D + D + 1],
                                         adj_f[:, j, t * P:(t + 1) * P], hu[:, j, 0:D + 1],
                                         start=(j == 0), stop=(j == T - 1))
                last.then_inc(msg_ready, 1)

        def gnn_out(b):
            transpose_xn(b * 2 + 1)

        def front(b, h, par, first_head=False):
            f = b * H + h
            if first_head:
                pe.wait_ge(xnT_copied, b * 2 + 2)
            for i in range(2):
                if i == 0 and not first_head:
                    pe.wait_ge(q_copied, f)
                if i == 1 and not first_head:
                    pe.wait_ge(sim_copied, f * 2)
                for t in (2 * i, 2 * i + 1):
                    last = pe.matmul(front_ps[i][:, (t % 2) * 256:(t % 2 + 1) * 256], x2nT[:, t * P:(t + 1) * P],
                                     w_sim[:, bass.ds(h * 256, 256)], start=True, stop=True)
                last.then_inc(sim_ready, 1)
            pe.wait_ge(wq_ready, f + 1)
            pe.wait_ge(sim_copied, f * 2 + 1)
            pe.matmul(front_ps[0][:, :], wq_head[:, :], x2nT[:, :], start=True, stop=True).then_inc(q_ready, 1)

        def step(b, h, par, gnn_too=False, last_head=False, last=False):
            s = b * H + h
            if last_head and not last:
                gnn_out(b + 1)
                front(b + 1, 0, 1 - par, first_head=True)
            elif not last:
                front(b, h + 1, 1 - par)

            def combine(t, k0, k1):
                end = last and t == T - 1
                if k0 == 0 and not end:
                    pe.wait_ge(gathered[t], s * (TOPK * 16) + TOPK * 16)
                if k0 == 0:
                    pe.wait_ge(diag_ready, s * T + t + 1)
                for k in range(k0, k1):
                    if end and k % (TOPK // QUARTERS) == 0:
                        pe.wait_ge(gathered_end[k * QUARTERS // TOPK], TOPK // QUARTERS * 16)
                    mm = pe.matmul(comb_ps[t % 2][:, 0:2 * D], diag[t % 2][:, k, :], got[t][:, k, :],
                                   start=(k == 0), stop=(k == TOPK - 1))
                if k1 == TOPK:
                    mm.then_inc(combined, 1)

            def key_transpose(t):
                pe.wait_ge(kv_copied, s * T + t + 1)
                pe.transpose(keyT_ps, kv[:, t, 0:D], ident[:, :]).then_inc(keyT_ready, 1)

            def scores(t):
                if t == 0:
                    pe.wait_ge(q_copied, s + 1)
                pe.wait_ge(keyT_copied, s * T + t + 1)
                pe.matmul(score_ps[:, 0:(t + 1) * P], qT[par][:, t * P:(t + 1) * P], keyT[:, 0:(t + 1) * P],
                          start=True, stop=True).then_inc(scored, 1)

            def prob_transpose(t):
                pe.wait_ge(prob_ready, s * T + t + 1)
                if t:
                    pe.wait_ge(added, s * T + t)
                for j in range(t + 1):
                    last = pe.transpose(probT_ps[:, j * P:(j + 1) * P], prob[:, j * P:(j + 1) * P], ident[:, :])
                last.then_inc(probT_ready, 1)

            def values(t):
                pe.wait_ge(probT_copied, s * T + t + 1)
                for j in range(t + 1):
                    last = pe.matmul(headT_ps, kv[:, j, D:2 * D], probT[:, j * P:(j + 1) * P],
                                     start=(j == 0), stop=(j == t))
                last.then_inc(headT_ready, 1)

            def project(t):
                pe.wait_ge(headT_copied, s * T + t + 1)
                pe.matmul(proj_ps, headT[:, :], wo_sb[:, bass.ds(h, 1), :].rearrange("p a n -> p (a n)"),
                          start=True, stop=True).then_inc(projected, 1)

            stages = (key_transpose, scores, prob_transpose, values, project)
            cuts = (0, 3, 5, 10, 13, TOPK)
            combine(0, 0, TOPK)
            for t in range(1, T):
                for stage, k0, k1 in zip(stages, cuts, cuts[1:]):
                    combine(t, k0, k1)
                    stage(t - 1)
                if gnn_too and t == 1:
                    pe.wait_ge(q_copied, s + 2)
                    gnn_hu(b + 1)
                if gnn_too and t == 2:
                    gnn_msg(b + 1)
            for stage in stages:
                stage(T - 1)

        def first():
            pe.wait_ge(consts, 3)
            pe.wait_ge(ones_ready, 1)
            pe.wait_ge(gnn_loaded, 3 * 16)
            gnn_hu(0)
            gnn_msg(0)
            fold()
            gnn_out(0)
            pe.wait_ge(heads_loaded, 2 * 16)
            front(0, 0, 0, first_head=True)

        schedule(pe, first, step)

    @block.scalar
    def _(act):
        def copy(dst, src, scale=1.0):
            return act.activation(dst, src, ACT.Copy, scale=scale)

        def fold():
            for g in range(SIDES * H // 4):
                act.wait_ge(fold_ready, g + 1)
                copy(w_sim[:, g * 512:(g + 1) * 512], fold_ps[g % 2][:, :]).then_inc(fold_copied, 1)

        def root(n):
            act.wait_ge(var_ready, n + 1)
            act.activation(sd[:, :], var[:, :], ACT.Sqrt).then_inc(sd_ready, 1)

        def gnn_hu(b):
            act.wait_ge(xnT_ready, b * 2 + 1)
            copy(xnT[:, :], front_ps[0][:, :]).then_inc(xnT_copied, 1)
            act.wait_ge(adj_loaded, b * 16 + 16)
            copy(adj_f[:, :, :], adj_i[:, :, :]).then_inc(adj_cast, 1)
            for i in range(2):
                act.wait_ge(hu_ready, b * 2 + i + 1)
                ps = front_ps[1 - i][:, :].rearrange("p (t c) -> p t c", t=2)
                copy(hu[:, 2 * i:2 * i + 2, 0:D], ps[:, :, 0:D])
                copy(hu[:, 2 * i:2 * i + 2, D + 1:], ps[:, :, D:2 * D]).then_inc(hu_copied, 1)

        def gnn_out(b):
            act.wait_ge(xnT_ready, b * 2 + 2)
            copy(x2nT[:, :], front_ps[0][:, :]).then_inc(xnT_copied, 1)

        def front(b, h, par, first=False):
            f = b * H + h
            if not first:
                act.wait_ge(q_ready, f)
                act.sem_inc(held, 1)
            copy(wq_head[:, :], wq_sb[:, bass.ds(h * D, D)]).then_inc(wq_ready, 1)
            for i in range(2):
                act.wait_ge(sim_ready, f * 2 + i + 1)
                if not first:
                    act.wait_ge(sim_used, f * T + (2 * i - 2))
                copy(sim[:, 2 * i:2 * i + 2, :], front_ps[i][:, :]).then_inc(sim_copied, 1)
            act.wait_ge(q_ready, f + 1)
            copy(qT[par][:, :], front_ps[0][:, :], scale=SCALE).then_inc(q_copied, 1)

        def weights(f, t, n):
            act.wait_ge(gap_ready, f * T + t + n)
            act.activation(wexp[:, t:t + n, :], gap[:, t:t + n, :], ACT.Exp).then_inc(wexp_ready, n)

        def first():
            root(0)
            gnn_hu(0)
            fold()
            root(1)
            gnn_out(0)
            act.wait_ge(heads_loaded, 2 * 16)
            front(0, 0, 0, first=True)
            for t, n in FIRST_TILES:
                weights(0, t, n)

        def step(b, h, par, gnn_too=False, last_head=False, last=False):
            s = b * H + h
            if last_head and not last:
                gnn_out(b + 1)
                front(b + 1, 0, 1 - par)
            elif not last:
                front(b, h + 1, 1 - par)
            if gnn_too:
                root(b * 2 + 2)

            def take_kv(t):
                act.wait_ge(combined, s * T + t + 1)
                copy(kv[:, t, :], comb_ps[t % 2][:, 0:2 * D]).then_inc(kv_copied, 1)

            def take_keyT(t):
                act.wait_ge(keyT_ready, s * T + t + 1)
                copy(keyT[:, t * P:(t + 1) * P], keyT_ps).then_inc(keyT_copied, 1)

            def exponent(t):
                act.wait_ge(neg_ready, s * T + t + 1)
                act.activation(prob[:, 0:(t + 1) * P], neg[:, 0:(t + 1) * P], ACT.Exp, bias=neg_max[:, :],
                               scale=-1.0, accum_out=prob_sum[:, :]).then_inc(prob_ready, 1)

            def take_probT(t):
                act.wait_ge(probT_ready, s * T + t + 1)
                copy(probT[:, 0:(t + 1) * P], probT_ps[:, 0:(t + 1) * P]).then_inc(probT_copied, 1)

            def take_headT(t):
                act.wait_ge(headT_ready, s * T + t + 1)
                copy(headT[:, :], headT_ps).then_inc(headT_copied, 1)

            def attend(t):
                take_keyT(t)
                exponent(t)
                take_probT(t)
                take_headT(t)

            for t in range(T):
                if t:
                    attend(t - 1)
                take_kv(t)
                if t == 1 and gnn_too:
                    gnn_hu(b + 1)
                if t in (1, 2) and not last:
                    weights(s + 1, 2 * t - 2, 2)
            attend(T - 1)
            if gnn_too:
                root(b * 2 + 3)

        schedule(act, first, step)

    @block.vector
    def _(dve):
        count = [0]

        def link(instruction):
            instruction.then_inc(chain, 1)
            count[0] += 1
            return count[0]

        def after(n):
            dve.wait_ge(chain, n)

        def restart():
            after(count[0])
            dve.sem_clear(chain)
            count[0] = 0

        def setup():
            dve.wait_ge(consts, 3)
            dve.tensor_copy(ident_ps, ident[:, :])
            for h in range(H):
                dve.memset(head_row[:, h:h + 1], float(h * ROWS))
            dve.tensor_copy(iota_ps, iota_i[:, :])
            after(link(dve.memset(hu[:, :, D:D + 1], 1.0)))
            dve.sem_inc(ones_ready, 1)
            restart()

        def layernorm(src, n):
            for t in range(T):
                a = link(dve.bn_stats(stats[:, t, :], src[:, t, :]))
            for t in range(T):
                after(a - T + 1 + t)
                c = link(dve.bn_aggr(meanvar[:, t, :], stats[:, t, :]))
            after(c)
            dve.tensor_scalar(var[:, :], meanvar[:, :, 1], EPS, None, ALU.add).then_inc(var_ready, 1)
            dve.wait_ge(sd_ready, n + 1)
            after(link(dve.reciprocal(rstd[:, :], sd[:, :])))
            after(link(dve.tensor_tensor(rstd2[:, :], rstd[:, :], rstd[:, :], ALU.mult)))
            after(link(dve.tensor_tensor(rstd2[:, :], rstd2[:, :], var[:, :], ALU.mult)))
            after(link(dve.tensor_scalar(rstd2[:, :], rstd2[:, :], -0.5, 1.5, ALU.mult, ALU.add)))
            after(link(dve.tensor_tensor(rstd[:, :], rstd[:, :], rstd2[:, :], ALU.mult)))
            for t in range(T):
                a = link(dve.tensor_scalar(xn[:, t, :], src[:, t, :], meanvar[:, t, 0:1], rstd[:, t:t + 1],
                                           ALU.subtract, ALU.mult))
            after(a)
            dve.sem_inc(xn_ready, 1)

        def gnn_in(b):
            dve.wait_ge(x_loaded, b * 16 + 16)
            dve.sem_inc(held, 1)
            layernorm(x_in, b * 2)

        def gnn_msg(b, first_batch=False):
            for i in range(2):
                dve.wait_ge(msg_ready, b * 2 + i + 1)
                ps = front_ps[1 - i][:, :].rearrange("p (t c) -> p t c", t=2)
                d, g = deg[:, 2 * i:2 * i + 2], degpos[:, 2 * i:2 * i + 2]
                a = link(dve.tensor_scalar(d, ps[:, :, D], 1.0, None, ALU.max))
                c = link(dve.tensor_scalar(g, ps[:, :, D], 0.0, None, ALU.is_gt))
                after(a)
                after(link(dve.reciprocal(d, d)))
                after(link(dve.tensor_tensor(d, d, g, ALU.mult)))
                for t in (2 * i, 2 * i + 1):
                    a = link(dve.scalar_tensor_tensor(upd[:, t, :], ps[:, t % 2, 0:D], deg[:, t:t + 1],
                                                      hu[:, t, D + 1:], ALU.mult, ALU.add))
            after(a)
            after(link(dve.tensor_tensor(upd[:, :, :], upd[:, :, :],
                                         bias_all[:, :].unsqueeze(1).broadcast_to([P, T, D]), ALU.add)))
            after(link(dve.scalar_tensor_tensor(x2[:, :, :], upd[:, :, :], 0.0, x_in[:, :, :], ALU.max, ALU.add)))
            dve.sem_inc(x_used, 1)
            if first_batch:
                link(dve.tensor_copy(acc[:, :, :], x2[:, :, :]))
            layernorm(x2, b * 2 + 1)

        def rank(f, t0, nt):
            dve.wait_ge(sim_copied, f * 2 + t0 // 2 + 1)
            dve.sem_inc(held, 1)
            lanes = [(t0 + u, p, 2 * u + p) for u in range(nt) for p in range(SIDES)]
            full = [sim[:, t, p * NKEYS:(p + 1) * NKEYS] for t, p, _ in lanes]
            rest = [sim_rest[:, r, :] for _, _, r in lanes]
            for n in range(5):
                for (t, p, r), src, left in zip(lanes, full, rest):
                    v, ix = top_v[:, t, p, :], top_i[:, t, p, :]
                    if n:
                        after(count[0] - len(lanes) + 1)
                    if n == 0:
                        link(dve.max(v[:, 0:8], src))
                    if n == 1:
                        link(dve.max_index(ix[:, 0:8], v[:, 0:8], src))
                    if n == 2:
                        link(dve.match_replace(left, v[:, 0:8], src, LOWEST))
                    if n == 3:
                        link(dve.max(v[:, 8:16], left))
                    if n == 4:
                        link(dve.max_index(ix[:, 8:16], v[:, 8:16], left))
            after(count[0])
            dve.sem_inc(sim_used, nt)

        def choose(f, t0, nt, h, par):
            these = slice(t0, t0 + nt)
            link(dve.tensor_copy(top_f[:, these, 0, :], top_i[:, these, 0, :]))
            c = link(dve.tensor_scalar(top_f[:, these, 1, :], top_i[:, these, 1, :], float(NKEYS),
                                       head_row[:, bass.ds(h, 1)], ALU.mult, ALU.add))
            for dst, src in ((cand, top_v), (cand_row, top_f)):
                if src is top_f:
                    after(c)
                for g, n in GROUPS:
                    w = RUN[g]
                    o = dst[:, these, START[g]:START[g] + n * w].rearrange("p t (a w) -> p t a w", a=n)
                    link(dve.tensor_tensor(o, src[:, these, 0, g:g + n].unsqueeze(3).broadcast_to([P, nt, n, w]),
                                           src[:, these, 1, 0:w].unsqueeze(2).broadcast_to([P, nt, n, w]), ALU.add))
            after(count[0])
            for n in range(5):
                for t in range(t0, t0 + nt):
                    if n:
                        after(count[0] - nt + 1)
                    v, ix = best[:, t, :], place[:, t, :]
                    if n == 0:
                        link(dve.max(v[:, 0:8], cand[:, t, :]))
                    if n == 1:
                        link(dve.max_index(ix[:, 0:8], v[:, 0:8], cand[:, t, :]))
                    if n == 2:
                        link(dve.match_replace(cand_rest[:, t, :], v[:, 0:8], cand[:, t, :], LOWEST))
                    if n == 3:
                        link(dve.max(v[:, 8:16], cand_rest[:, t, :]))
                    if n == 4:
                        link(dve.max_index(ix[:, 8:16], v[:, 8:16], cand_rest[:, t, :]))
            dve.tensor_tensor(gap[:, these, :], best[:, these, :], best[:, these, 0:1].broadcast_to([P, nt, TOPK]),
                              ALU.subtract).then_inc(gap_ready, nt)
            after(count[0])
            n = nt * TOPK
            hot = onehot[:, 0:nt, :, :]
            flat = hot.rearrange("p t k c -> p (t k) c")
            after(link(dve.tensor_tensor(
                flat, place[:, these, :].rearrange("p t k -> p (t k)").unsqueeze(2).broadcast_to([P, n, NCAND]),
                iota_ps.unsqueeze(1).broadcast_to([P, n, NCAND]), ALU.is_equal)))
            after(link(dve.tensor_tensor(hot, hot,
                                         cand_row[:, these, :].unsqueeze(2).broadcast_to([P, nt, TOPK, NCAND]),
                                         ALU.mult)))
            with nc.allow_low_precision(reason="the sum of one row number and zeros"):
                dve.tensor_reduce(rows[par][:, t0 * TOPK:t0 * TOPK + n], flat, AX.X, ALU.add).then_inc(rows_ready, nt)
            dve.wait_ge(wexp_ready, f * T + t0 + nt)
            after(link(dve.tensor_reduce(wsum[:, these], wexp[:, these, :], AX.X, ALU.add)))
            after(link(dve.reciprocal(wsum[:, these], wsum[:, these])))
            after(link(dve.tensor_tensor(wts[par][:, these, :], wexp[:, these, :],
                                         wsum[:, these].unsqueeze(2).broadcast_to([P, nt, TOPK]), ALU.mult)))

        def first():
            setup()
            gnn_in(0)
            gnn_msg(0, first_batch=True)
            for t, n in FIRST_TILES:
                rank(0, t, n)
                choose(0, t, n, 0, 0)
            restart()

        def step(b, h, par, gnn_too=False, last_head=False, last=False):
            s = b * H + h

            def weigh(t):
                if t >= 2:
                    dve.wait_ge(combined, s * T + t - 1)
                dve.tensor_tensor(diag[t % 2][:, :, :], ident_ps.unsqueeze(1).broadcast_to([P, TOPK, P]),
                                  wts[par][:, t, :].unsqueeze(2).broadcast_to([P, TOPK, P]),
                                  ALU.mult).then_inc(diag_ready, 1)

            def negate(t):
                dve.wait_ge(scored, s * T + t + 1)
                dve.sem_inc(held, 1)
                n = (t + 1) * P
                dve.tensor_tensor_reduce(out=neg[:, 0:n], in0=score_ps[:, 0:n], in1=mask[:, N - n:N], scale=-1.0,
                                         scalar=-LOWEST, op0=ALU.add, op1=ALU.min,
                                         accum_out=neg_max[:, :]).then_inc(neg_ready, 1)

            def add(t):
                dve.wait_ge(prob_ready, s * T + t + 1)
                a = link(dve.reciprocal(prob_inv[:, :], prob_sum[:, :]))
                dve.wait_ge(projected, s * T + t + 1)
                after(a)
                if last_head:
                    if t == 0:
                        dve.wait_ge(fin_free, b + 1)
                    a = link(dve.scalar_tensor_tensor(fin[:, t, :], proj_ps, prob_inv[:, :], acc[:, t, :],
                                                      ALU.mult, ALU.add))
                    after(a)
                    dve.sem_inc(fin_ready, 1)
                    dve.sem_inc(added, 1)
                    if not last:
                        link(dve.tensor_copy(acc[:, t, :], x2[:, t, :]))
                else:
                    a = link(dve.scalar_tensor_tensor(acc[:, t, :], proj_ps, prob_inv[:, :], acc[:, t, :],
                                                      ALU.mult, ALU.add))
                    after(a)
                    dve.sem_inc(added, 1)

            next_h = 0 if last_head else h + 1
            weigh(0)
            weigh(1)
            if not last:
                for t, n in PAIRS:
                    rank(s + 1, t, n)
            if gnn_too:
                gnn_in(b + 1)
            negate(0)
            add(0)
            weigh(2)
            if not last:
                choose(s + 1, *PAIRS[0], next_h, 1 - par)
            negate(1)
            add(1)
            weigh(3)
            if not last:
                choose(s + 1, *PAIRS[1], next_h, 1 - par)
            negate(2)
            add(2)
            negate(3)
            add(3)
            if gnn_too:
                gnn_msg(b + 1)
            restart()

        schedule(dve, first, step)

    block_ctx.__exit__(None, None, None)


def kernel(x, adj, L0_gnn_W_msg, L0_gnn_W_upd, L0_gnn_bias, L0_ffn_Wq_pk, L0_ffn_pk_keys, L0_ffn_Wq,
           L0_ffn_keys_table, L0_ffn_values_table, L0_ffn_Wo):
    import numpy as np
    import concourse.bacc as bacc
    from concourse.bass_utils import run_bass_kernel_spmd as run

    c = np.ascontiguousarray
    wqpk = np.asarray(L0_ffn_Wq_pk).reshape(D, SIDES, H, DKEY)
    keys = np.asarray(L0_ffn_pk_keys)
    arrays = {
        "x": c(x), "adj": c(adj), "w_msg": c(L0_gnn_W_msg), "w_upd": c(L0_gnn_W_upd), "bias": c(L0_gnn_bias),
        "wqpk_t": c(wqpk.transpose(3, 2, 1, 0).reshape(DKEY, H * SIDES * D)),
        "keys_t": c(keys.transpose(3, 2, 0, 1).reshape(DKEY, H * SIDES * NKEYS)),
        "wq": c(L0_ffn_Wq),
        "table": c(np.concatenate([np.asarray(L0_ffn_keys_table), np.asarray(L0_ffn_values_table)], axis=1)),
        "wo": c(L0_ffn_Wo),
    }
    nc = bacc.Bacc("TRN2", target_bir_lowering=False, num_devices=1)
    args = [nc.dram_tensor(f"in_{n}", a.shape, mybir.dt.from_np(a.dtype), kind="ExternalInput").ap()
            for n, a in arrays.items()]
    out = nc.dram_tensor("out", (B, N, D), F32, kind="ExternalOutput").ap()
    program(nc, *args, out)
    r = run(nc, [{f"in_{n}": a for n, a in arrays.items()}], core_ids=[0])
    return np.asarray(r.results[0]["out"])
```
